# Optimizing a Trainium2 kernel written in Bass

```python
import numpy as np
import jax
import jax.numpy as jnp

def _softmax(x, axis=-1):
    return jax.nn.softmax(x, axis=axis)

def _gelu(x):
    return jax.nn.gelu(x, approximate=True)

def _silu(x):
    return jax.nn.silu(x)

def _sigmoid(x):
    return jax.nn.sigmoid(x)

def _layernorm(x, axis=-1, eps=1e-05):
    m = jnp.mean(x, axis=axis, keepdims=True)
    v = jnp.var(x, axis=axis, keepdims=True)
    return (x - m) / jnp.sqrt(v + eps)

def _scatter_add(tgt, idx, src, axis=0):
    return tgt.at[idx].add(src)

def _segment_sum(src, seg, n):
    return jax.ops.segment_sum(src, seg, n)
kernel_name = 'mk_sandwich_d2_jaxref_r8_d471f6'

def setup_inputs(seed: int=0):
    np.random.seed(seed)
    _w = jnp.asarray

    def _L0_attn_setup():
        import jax, jax.numpy as jnp
        import numpy as np
        DIM = 128
        HEADS = 16
        DIM_HEAD = DIM // HEADS
        B, N = (4, 128)
        key = jax.random.key(seed)
        ks = jax.random.split(key, 8)
        s = 1.0 / np.sqrt(DIM)
        inp = {'x': jax.random.normal(ks[0], (B, N, DIM), dtype=jnp.float32), 'Wq': jax.random.normal(ks[1], (DIM, DIM), dtype=jnp.float32) * s, 'Wk': jax.random.normal(ks[2], (DIM, DIM), dtype=jnp.float32) * s, 'Wv': jax.random.normal(ks[3], (DIM, DIM), dtype=jnp.float32) * s, 'Wproj': jax.random.normal(ks[4], (DIM, DIM), dtype=jnp.float32) * s, 'bproj': jnp.zeros((DIM,), dtype=jnp.float32), 'Wpre': jax.random.normal(ks[5], (DIM, DIM), dtype=jnp.float32) * s, 'bpre': jnp.zeros((DIM,), dtype=jnp.float32), 'pi': jnp.full((1,), 0.5, dtype=jnp.float32)}
        return inp
    _L0_attn_in = _L0_attn_setup()

    def _L0_ffn_setup():
        import jax, jax.numpy as jnp
        import numpy as np
        import math
        DMODEL = 128
        DFF = 512
        NUM_EXPERTS = 8
        TOPK = 2
        CAP_FACTOR = 1.25
        EPS = 1.1920929e-07

        def _trunc_normal(key, shape, fan_in, scale=1.0):
            std = scale * (1.0 / fan_in) ** 0.5
            return jax.random.truncated_normal(key, -2.0, 2.0, shape, jnp.float32) * std
        key = jax.random.key(seed)
        ks = jax.random.split(key, 5)
        return {'x': jax.random.normal(ks[0], (2, 256, DMODEL), jnp.float32), 'router_weight': _trunc_normal(ks[1], (NUM_EXPERTS, DMODEL), DMODEL), 'ff_pre_act_weight': _trunc_normal(ks[2], (NUM_EXPERTS, DFF, DMODEL), DMODEL), 'gate_weight': _trunc_normal(ks[3], (NUM_EXPERTS, DFF, DMODEL), DMODEL), 'ff_post_act_weight': _trunc_normal(ks[4], (NUM_EXPERTS, DMODEL, DFF), DFF)}
    _L0_ffn_in = _L0_ffn_setup()

    def _L1_attn_setup():
        import jax, jax.numpy as jnp
        import numpy as np
        H = 16
        G = 4
        MAX_POS = 128
        key = jax.random.key(seed)
        ks = jax.random.split(key, 6)
        B, T, D = (8, 128, 128)
        hd = D // H
        s = 0.02
        return {'x': jax.random.normal(ks[0], (B, T, D), jnp.float32), 'Wq': jax.random.normal(ks[1], (D, D), jnp.float32) * s, 'Wk': jax.random.normal(ks[2], (hd * G, D), jnp.float32) * s, 'Wv': jax.random.normal(ks[3], (hd * G, D), jnp.float32) * s, 'Wo': jax.random.normal(ks[4], (D, D), jnp.float32) * s, 'E': jax.random.normal(ks[5], (2 * MAX_POS - 1, hd), jnp.float32) * s}
    _L1_attn_in = _L1_attn_setup()

    def _L1_ffn_setup():
        import jax, jax.numpy as jnp
        import numpy as np
        TOP_K = 32
        TEMPERATURE = 1.0
        PARAM_SCALE = 0.02

        def _compose_weight(logits, A, B):
            vals, idx = jax.lax.top_k(logits, TOP_K)
            w = jax.nn.softmax(vals / TEMPERATURE)
            A_sel = A[idx]
            B_sel = B[idx]
            return jnp.einsum('k,kir,kro->io', w, A_sel, B_sel)
        key = jax.random.key(seed)
        ks = jax.random.split(key, 7)
        B, S, D, F, P, R = (2, 128, 128, 512, 32, 64)
        x = jax.random.normal(ks[0], (B, S, D), dtype=jnp.float32)
        fc1_A = jax.random.normal(ks[1], (P, D, R), dtype=jnp.float32) * PARAM_SCALE
        fc1_B = jax.random.normal(ks[2], (P, R, F), dtype=jnp.float32) * PARAM_SCALE
        fc2_A = jax.random.normal(ks[3], (P, F, R), dtype=jnp.float32) * PARAM_SCALE
        fc2_B = jax.random.normal(ks[4], (P, R, D), dtype=jnp.float32) * PARAM_SCALE
        fc1_logits = jax.random.normal(ks[5], (P,), dtype=jnp.float32)
        fc2_logits = jax.random.normal(ks[6], (P,), dtype=jnp.float32)
        return {'x': x, 'fc1_A': fc1_A, 'fc1_B': fc1_B, 'fc2_A': fc2_A, 'fc2_B': fc2_B, 'fc1_logits': fc1_logits, 'fc2_logits': fc2_logits}
    _L1_ffn_in = _L1_ffn_setup()
    _d = {'L0_attn_x': _L0_attn_in['x'], 'L0_attn_Wq': _L0_attn_in['Wq'], 'L0_attn_Wk': _L0_attn_in['Wk'], 'L0_attn_Wv': _L0_attn_in['Wv'], 'L0_attn_Wproj': _L0_attn_in['Wproj'], 'L0_attn_bproj': _L0_attn_in['bproj'], 'L0_attn_Wpre': _L0_attn_in['Wpre'], 'L0_attn_bpre': _L0_attn_in['bpre'], 'L0_attn_pi': _L0_attn_in['pi'], 'L0_ffn_router_weight': _L0_ffn_in['router_weight'], 'L0_ffn_ff_pre_act_weight': _L0_ffn_in['ff_pre_act_weight'], 'L0_ffn_gate_weight': _L0_ffn_in['gate_weight'], 'L0_ffn_ff_post_act_weight': _L0_ffn_in['ff_post_act_weight'], 'L1_attn_Wq': _L1_attn_in['Wq'], 'L1_attn_Wk': _L1_attn_in['Wk'], 'L1_attn_Wv': _L1_attn_in['Wv'], 'L1_attn_Wo': _L1_attn_in['Wo'], 'L1_attn_E': _L1_attn_in['E'], 'L1_ffn_fc1_A': _L1_ffn_in['fc1_A'], 'L1_ffn_fc1_B': _L1_ffn_in['fc1_B'], 'L1_ffn_fc2_A': _L1_ffn_in['fc2_A'], 'L1_ffn_fc2_B': _L1_ffn_in['fc2_B'], 'L1_ffn_fc1_logits': _L1_ffn_in['fc1_logits'], 'L1_ffn_fc2_logits': _L1_ffn_in['fc2_logits']}
    _x0 = _d['L0_attn_x']
    _d['L0_attn_x'] = jax.random.normal(jax.random.fold_in(jax.random.key(seed), 1), (2, 1024, 128), dtype=_x0.dtype)
    del _x0
    return _d

def reference(L0_attn_x, L0_attn_Wq, L0_attn_Wk, L0_attn_Wv, L0_attn_Wproj, L0_attn_bproj, L0_attn_Wpre, L0_attn_bpre, L0_attn_pi, L0_ffn_router_weight, L0_ffn_ff_pre_act_weight, L0_ffn_gate_weight, L0_ffn_ff_post_act_weight, L1_attn_Wq, L1_attn_Wk, L1_attn_Wv, L1_attn_Wo, L1_attn_E, L1_ffn_fc1_A, L1_ffn_fc1_B, L1_ffn_fc2_A, L1_ffn_fc2_B, L1_ffn_fc1_logits, L1_ffn_fc2_logits):

    def _L0_attn_ref(x, Wq, Wk, Wv, Wproj, bproj, Wpre, bpre, pi):
        import jax, jax.numpy as jnp
        import numpy as np
        DIM = 128
        HEADS = 16
        DIM_HEAD = DIM // HEADS
        B, N = (4, 128)
        b, n, c = x.shape
        h, dh = (HEADS, DIM_HEAD)
        residual = x
        pre = jax.nn.silu(x @ Wpre + bpre)
        logits = jnp.einsum('bnc,bmc->bnm', pre, pre) / jnp.sqrt(jnp.float32(c))
        q = (x @ Wq).reshape(b, n, h, dh).transpose(0, 2, 1, 3)
        k = (x @ Wk).reshape(b, n, h, dh).transpose(0, 2, 1, 3)
        v = (x @ Wv).reshape(b, n, h, dh).transpose(0, 2, 1, 3)
        score = jnp.einsum('bhnd,bhmd->bhnm', q, k) / jnp.sqrt(jnp.float32(dh))
        final_logits = pi[0] * logits[:, None, :, :] + score
        attn = jax.nn.softmax(final_logits, axis=-1)
        out = jnp.einsum('bhnm,bhmd->bhnd', attn, v)
        out = out.transpose(0, 2, 1, 3).reshape(b, n, h * dh)
        out = out @ Wproj + bproj
        return out + residual

    def _L0_ffn_ref(x, router_weight, ff_pre_act_weight, gate_weight, ff_post_act_weight):
        import jax, jax.numpy as jnp
        import numpy as np
        import math
        DMODEL = 128
        DFF = 512
        NUM_EXPERTS = 8
        TOPK = 2
        CAP_FACTOR = 1.25
        EPS = 1.1920929e-07

        def _trunc_normal(key, shape, fan_in, scale=1.0):
            std = scale * (1.0 / fan_in) ** 0.5
            return jax.random.truncated_normal(key, -2.0, 2.0, shape, jnp.float32) * std
        orig_shape = x.shape
        h = x.reshape(-1, DMODEL)
        T = h.shape[0]
        logits = jnp.einsum('th,eh->te', h, router_weight)
        probs = jax.nn.softmax(logits.astype(jnp.float32), axis=-1)
        topk_probs, selected = jax.lax.top_k(probs, TOPK)
        topk_probs = topk_probs / jnp.maximum(topk_probs.sum(-1, keepdims=True), EPS)
        flat_tokens = jnp.repeat(jnp.arange(T), TOPK)
        flat_experts = selected.reshape(-1)
        flat_weights = topk_probs.reshape(-1)
        A = T * TOPK
        capacity = max(1, math.ceil(CAP_FACTOR * A / NUM_EXPERTS))
        weight_order = jnp.argsort(-flat_weights, stable=True)
        grouped_order = jnp.argsort(flat_experts[weight_order], stable=True)
        sort_order = weight_order[grouped_order]
        se = flat_experts[sort_order]
        st = flat_tokens[sort_order]
        sw = flat_weights[sort_order]
        counts = jnp.bincount(se, length=NUM_EXPERTS)
        offsets = jnp.cumsum(counts) - counts
        slot = jnp.arange(A) - offsets[se]
        keep = slot < capacity
        sw = jnp.where(keep, sw, 0.0)
        token_wsum = jnp.zeros(T, jnp.float32).at[st].add(sw)
        kept_w = sw / jnp.maximum(token_wsum[st], EPS)
        FC = NUM_EXPERTS * capacity
        dispatch = jnp.where(keep, se * capacity + slot, FC)
        expert_inputs = jnp.zeros((FC + 1, DMODEL), x.dtype).at[dispatch].set(h[st])
        expert_inputs = expert_inputs[:FC].reshape(NUM_EXPERTS, capacity, DMODEL)
        pre = jnp.einsum('ech,edh->ecd', expert_inputs, ff_pre_act_weight)
        gate = jnp.einsum('ech,edh->ecd', expert_inputs, gate_weight)
        expert_out = jnp.einsum('ecd,ehd->ech', pre * jax.nn.silu(gate), ff_post_act_weight)
        eo_flat = jnp.concatenate([expert_out.reshape(FC, DMODEL), jnp.zeros((1, DMODEL), x.dtype)], axis=0)
        updates = eo_flat[dispatch] * kept_w.astype(x.dtype)[:, None]
        out = jnp.zeros((T, DMODEL), x.dtype).at[st].add(updates)
        return out.reshape(orig_shape)

    def _L1_attn_ref(x, Wq, Wk, Wv, Wo, E):
        import jax, jax.numpy as jnp
        import numpy as np
        H = 16
        G = 4
        MAX_POS = 128
        B, T, D = x.shape
        hd = D // H
        r = H // G
        q = (x @ Wq.T).reshape(B, T, H, hd).transpose(0, 2, 1, 3)
        k = (x @ Wk.T).reshape(B, T, G, hd)
        v = (x @ Wv.T).reshape(B, T, G, hd)
        k = jnp.repeat(k, r, axis=2).transpose(0, 2, 1, 3)
        v = jnp.repeat(v, r, axis=2).transpose(0, 2, 1, 3)
        q = q * (1.0 / hd) ** 0.5
        scores = jnp.einsum('bhqd,bhkd->bhqk', q, k)
        pos = jnp.arange(T)
        dist = jnp.clip(pos[None, :] - pos[:, None], -MAX_POS + 1, MAX_POS - 1) + MAX_POS - 1
        R = E[dist]
        bias = jnp.einsum('bhqd,kqd->bhqk', q, R)
        scores = scores + bias
        attn = jax.nn.softmax(scores, axis=-1)
        out = jnp.einsum('bhqk,bhkd->bhqd', attn, v)
        out = out.transpose(0, 2, 1, 3).reshape(B, T, D)
        return out @ Wo.T

    def _L1_ffn_ref(x, fc1_A, fc1_B, fc2_A, fc2_B, fc1_logits, fc2_logits):
        import jax, jax.numpy as jnp
        import numpy as np
        TOP_K = 32
        TEMPERATURE = 1.0
        PARAM_SCALE = 0.02

        def _compose_weight(logits, A, B):
            vals, idx = jax.lax.top_k(logits, TOP_K)
            w = jax.nn.softmax(vals / TEMPERATURE)
            A_sel = A[idx]
            B_sel = B[idx]
            return jnp.einsum('k,kir,kro->io', w, A_sel, B_sel)
        W1 = _compose_weight(fc1_logits, fc1_A, fc1_B)
        W2 = _compose_weight(fc2_logits, fc2_A, fc2_B)
        h = jax.nn.gelu(jnp.einsum('bsd,df->bsf', x, W1))
        return jnp.einsum('bsf,fd->bsd', h, W2)
    x = L0_attn_x
    x = x + _layernorm(_L0_attn_ref(_layernorm(x, axis=-1), L0_attn_Wq, L0_attn_Wk, L0_attn_Wv, L0_attn_Wproj, L0_attn_bproj, L0_attn_Wpre, L0_attn_bpre, L0_attn_pi), axis=-1)
    x = x + _layernorm(_L0_ffn_ref(_layernorm(x, axis=-1), L0_ffn_router_weight, L0_ffn_ff_pre_act_weight, L0_ffn_gate_weight, L0_ffn_ff_post_act_weight), axis=-1)
    x = x + _layernorm(_L1_attn_ref(_layernorm(x, axis=-1), L1_attn_Wq, L1_attn_Wk, L1_attn_Wv, L1_attn_Wo, L1_attn_E), axis=-1)
    x = x + _layernorm(_L1_ffn_ref(_layernorm(x, axis=-1), L1_ffn_fc1_A, L1_ffn_fc1_B, L1_ffn_fc2_A, L1_ffn_fc2_B, L1_ffn_fc1_logits, L1_ffn_fc2_logits), axis=-1)
    return x

_drawn_inputs = setup_inputs


def setup_inputs(seed=0):
    import zlib

    import numpy as np

    out = dict(_drawn_inputs(seed))
    spreads = {'L0_attn_bproj': (0.0, 0.1), 'L0_attn_bpre': (0.0, 0.629)}
    factors = {'L1_attn_E': 64.0,
     'L1_ffn_fc1_A': 5.594,
     'L1_ffn_fc1_B': 5.519,
     'L1_ffn_fc2_A': 5.442,
     'L1_ffn_fc2_B': 5.543,
     'L1_ffn_fc1_logits': 8.0,
     'L1_ffn_fc2_logits': 7.001}
    for name, (base, spread) in spreads.items():
        noise = np.random.default_rng([zlib.crc32(name.encode()), seed]).standard_normal(out[name].shape)
        drawn = base * np.exp(spread * noise) if base else spread * noise
        out[name] = jnp.asarray(drawn.astype(out[name].dtype))
    for name, factor in factors.items():
        out[name] = (out[name] * factor).astype(out[name].dtype)
    return out
```

```python
from contextlib import ExitStack, contextmanager

import concourse.bass as bass
from concourse import mybir
from concourse.alu_op_type import AluOpType as ALU

P = 128
B, N, C = 2, 1024, 128
TOK = B * N
NT = TOK // P
QT_N = N // P
H, DH = 16, 8
SPLIT = 3
KR = SPLIT * SPLIT * DH
E, DFF, TOPK = 8, 512, 2
CAP = -(-5 * TOK * TOPK // (4 * E))
FT = DFF // P
CH = 512
NCH = TOK // CH
TC = CH // P
EPS_LN = 1e-5
EPS_MOE = 1.1920929e-07
BAND = 512
RANK_ROWS = 32 * 64
KT_C = RANK_ROWS // P
HI = 16
FAR = 1e30
F32 = mybir.dt.float32
BF16 = mybir.dt.bfloat16
ACT = mybir.ActivationFunctionType
AX = mybir.AxisListType.X
SCORE_SCALE = DH ** -0.5


class Chain:

    def __init__(self, eng, sem):
        self.eng, self.sem, self.n = eng, sem, 0

    def __call__(self, ins):
        self.n += 1
        ins.then_inc(self.sem, 1)
        self.eng.wait_ge(self.sem, self.n)


class Phase:

    def __init__(self, nc, tag):
        self.nc, self.tag, self.ctx, self.sems = nc, tag, ExitStack(), []

    def sb(self, name, shape, dt=F32):
        return self.ctx.enter_context(self.nc.sbuf_tensor(f"{self.tag}_{name}", shape, dt))

    def pb(self, name, shape, dt=F32):
        return self.ctx.enter_context(self.nc.psum_tensor(f"{self.tag}_{name}", shape, dt))

    def sem(self, name):
        s = self.nc.alloc_semaphore(f"{self.tag}_{name}")
        self.sems.append(s)
        return s


@contextmanager
def phase(nc, tag):
    ph = Phase(nc, tag)
    yield ph
    nc.clear_and_free_semaphores(ph.sems)
    nc.all_engine_barrier()
    ph.ctx.close()


def spread(ap, shape):
    return ap.to_broadcast(shape)


def layer_norm(nc, tag, src, dst=None, add_to=None):
    with phase(nc, tag) as ph:
        normed = ph.sb("normed", [P, NT, C]) if dst is None else dst
        stats, agg = ph.sb("stats", [P, NT, 6]), ph.sb("agg", [P, NT, 2])
        var, rstd = ph.sb("var", [P, NT]), ph.sb("rstd", [P, NT])
        s_var, s_std, s_own = ph.sem("var"), ph.sem("std"), ph.sem("own")
        with nc.Block() as block:

            @block.vector
            def _(dve):
                own = Chain(dve, s_own)
                for t in range(NT):
                    last = nc.vector.bn_stats(stats[:, t, :], src[:, t, :])
                own(last)
                for t in range(NT):
                    last = nc.vector.bn_aggr(agg[:, t, :], stats[:, t, :])
                own(last)
                nc.vector.tensor_scalar(var[:], agg[:, :, 1], EPS_LN, None, ALU.add).then_inc(s_var, 1)
                dve.wait_ge(s_std, 1)
                own(nc.vector.reciprocal(rstd[:], var[:]))
                for t in range(NT):
                    last = nc.vector.tensor_scalar(normed[:, t, :], src[:, t, :], agg[:, t, 0:1], rstd[:, t:t + 1],
                                                   ALU.subtract, ALU.mult)
                own(last)
                if add_to is not None:
                    own(nc.vector.tensor_tensor(add_to[:], add_to[:], normed[:], ALU.add))

            @block.scalar
            def _(act):
                act.wait_ge(s_var, 1)
                nc.scalar.activation(var[:], var[:], ACT.Sqrt).then_inc(s_std, 1)


def split(nc, own, f, parts):
    for i in range(SPLIT):
        own(nc.vector.tensor_copy(parts[:, i], f))
        if i < SPLIT - 1:
            own(nc.vector.tensor_tensor(f, f, parts[:, i], ALU.subtract))


def project(nc, tag, b, xn, w, gkv, QT, KT, V, idf, idb, pre=None, efar=None):
    nvar = 3 if efar is not None else 1
    wide, kw = H * DH, gkv * DH
    nf, nk, width = wide + nvar * kw, nvar * gkv, wide + 2 * kw
    with phase(nc, tag) as ph:
        xT = ph.sb("xT", [P, 2, P])
        f = ph.sb("f", [P, 2, nf])
        parts = ph.sb("parts", [P, 2, SPLIT, nf], BF16)
        Qx = ph.sb("Qx", [P, 2, H, SPLIT, SPLIT, DH], BF16)
        Kx = ph.sb("Kx", [P, 2, nk, SPLIT, SPLIT, DH], BF16)
        psT = ph.pb("psT", [P, 2, 512])
        psQ = ph.pb("psQ", [P, 2, 512])
        psX = ph.pb("psX", [P, 4, 8, P], BF16)
        (s_t, s_xT, s_qkv, s_pm, s_pre, s_v, s_f, s_split, s_qx, s_kx, s_xq, s_xk, s_eq, s_ek, s_own) = (
            ph.sem(n) for n in "t xT qkv pm pre v f split qx kx xq xk eq ek own".split())
        with nc.Block() as block:

            @block.tensor
            def _(pe):
                def rows(n):
                    s = n % 2
                    if n >= 2:
                        pe.wait_ge(s_pre if pre else s_xT, n - 1)
                    nc.tensor.transpose(psT[:, s, 0:P], xn[:, b * QT_N + n, :], idf[:]).then_inc(s_t, 1)
                    pe.wait_ge(s_xT, n + 1)
                    if n >= 2:
                        pe.wait_ge(s_v, n - 1)
                    nc.tensor.matmul(psQ[:, s, 0:width], xT[:, s, :], w[:], start=True, stop=True).then_inc(s_qkv, 1)
                    if pre:
                        nc.tensor.matmul(psT[:, s, P:2 * P], pre[0][:], xT[:, s, :], start=True, stop=True).then_inc(s_pm, 1)

                def across(n):
                    s = n % 2
                    pe.wait_ge(s_qx, n + 1)
                    if n:
                        pe.wait_ge(s_eq, n)
                    for h in range(H):
                        last = nc.tensor.transpose(psX[0:KR, h // 8, h % 8, :], Qx[:, s, h].rearrange("p i j d -> p (i j d)"), idb[:])
                    last.then_inc(s_xq, 1)
                    pe.wait_ge(s_kx, n + 1)
                    if n:
                        pe.wait_ge(s_ek, n)
                    for k in range(nk):
                        last = nc.tensor.transpose(psX[0:KR, 2 + k // 8, k % 8, :], Kx[:, s, k].rearrange("p i j d -> p (i j d)"), idb[:])
                    last.then_inc(s_xk, 1)

                for n in range(QT_N + 1):
                    if n < QT_N:
                        rows(n)
                    if n:
                        across(n - 1)

            @block.scalar
            def _(act):
                for n in range(QT_N + 1):
                    s = n % 2
                    if n < QT_N:
                        act.wait_ge(s_t, n + 1)
                        nc.scalar.activation(xT[:, s, :], psT[:, s, 0:P], ACT.Copy).then_inc(s_xT, 1)
                        act.wait_ge(s_f, n + 1)
                        nc.scalar.activation(V[:, n, :, 0:DH], psQ[:, s, wide + kw:width].rearrange("p (g d) -> p g d", d=DH),
                                             ACT.Copy).then_inc(s_v, 1)
                        if pre:
                            act.wait_ge(s_pm, n + 1)
                            nc.scalar.activation(pre[2][:, n * P:(n + 1) * P], psT[:, s, P:2 * P], ACT.Silu,
                                                 bias=pre[1][:, 0:1]).then_inc(s_pre, 1)
                    if n:
                        act.wait_ge(s_xq, n)
                        nc.scalar.activation(QT[0:KR, :, (n - 1) * P:n * P], psX[0:KR, 0:2].rearrange("p a h t -> p (a h) t"),
                                             ACT.Copy).then_inc(s_eq, 1)

            @block.vector
            def _(dve):
                own = Chain(dve, s_own)
                for n in range(QT_N + 1):
                    s = n % 2
                    if n < QT_N:
                        dve.wait_ge(s_qkv, n + 1)
                        own(nc.vector.tensor_scalar(f[:, s, 0:wide], psQ[:, s, 0:wide], -SCORE_SCALE, None, ALU.mult))
                        if efar is not None:
                            for j in range(2):
                                own(nc.vector.tensor_tensor(f[:, s, wide + (j + 1) * kw:wide + (j + 2) * kw],
                                                            psQ[:, s, wide:wide + kw], efar[:, j, :], ALU.add))
                        nc.vector.tensor_copy(f[:, s, wide:wide + kw], psQ[:, s, wide:wide + kw]).then_inc(s_f, 1)
                        dve.wait_ge(s_f, n + 1)
                        if n >= 2:
                            dve.wait_ge(s_kx, n - 1)
                        split(nc, own, f[:, s, :], parts[:, s])
                        nc.vector.engine_nop().then_inc(s_split, 1)
                        if n >= 2:
                            dve.wait_ge(s_xq, n - 1)
                        for i in range(SPLIT):
                            last = nc.vector.tensor_copy(
                                Qx[:, s, :, i], spread(parts[:, s, i, 0:wide].rearrange("p (h d) -> p h d", d=DH).unsqueeze(2),
                                                       [P, H, SPLIT, DH]))
                        last.then_inc(s_qx, 1)
                    if n:
                        dve.wait_ge(s_xk, n)
                        nc.vector.tensor_copy(
                            KT[0:KR, :, (n - 1) * P:n * P],
                            psX[0:KR, 2:4].rearrange("p a h t -> p (a h) t")[:, 0:nk, :]).then_inc(s_ek, 1)

            @block.gpsimd
            def _(pool):
                for n in range(QT_N):
                    s = n % 2
                    pool.wait_ge(s_split, n + 1)
                    if n >= 2:
                        pool.wait_ge(s_xk, n - 1)
                    for j in range(SPLIT):
                        last = nc.gpsimd.tensor_copy(
                            Kx[:, s, :, :, j], spread(parts[:, s, j, wide:nf].rearrange("p (g d) -> p g d", d=DH).unsqueeze(2),
                                                      [P, nk, SPLIT, DH]))
                    last.then_inc(s_kx, 1)


def shared_logits(nc, tag, preT, negpi, L):
    with phase(nc, tag) as ph:
        ps = ph.pb("ps", [P, 2, N])
        s_mm, s_even, s_odd = ph.sem("mm"), ph.sem("even"), ph.sem("odd")
        with nc.Block() as block:

            @block.tensor
            def _(pe):
                for t in range(QT_N):
                    if t >= 2:
                        pe.wait_ge(s_odd if t % 2 else s_even, t // 2)
                    for c in range(N // 512):
                        last = nc.tensor.matmul(ps[:, t % 2, c * 512:(c + 1) * 512], preT[:, t * P:(t + 1) * P],
                                                preT[:, c * 512:(c + 1) * 512], start=True, stop=True)
                    last.then_inc(s_mm, 1)

            @block.scalar
            def _(act):
                for t in range(0, QT_N, 2):
                    act.wait_ge(s_mm, t + 1)
                    nc.scalar.activation(L[:, t, :], ps[:, 0, :], ACT.Copy, scale=negpi[:, 0:1]).then_inc(s_even, 1)

            @block.vector
            def _(dve):
                for t in range(1, QT_N, 2):
                    dve.wait_ge(s_mm, t + 1)
                    nc.vector.tensor_scalar(L[:, t, :], ps[:, 1, :], negpi[:, 0:1], None, ALU.mult).then_inc(s_odd, 1)


def attend(nc, tag, b, QT, KT, gkv, V, A, attn, con, segments, rel=None):
    GS = 4
    RPT = H // gkv
    idf, fold = con["idf"], con["fold"]
    with phase(nc, tag) as ph:
        Z = ph.sb("Z", [P, 2, N])
        Pt = ph.sb("Pt", [P, 2, N])
        m = ph.sb("m", [P, 2])
        touch = ph.sb("touch", [P, 3, QT_N])
        touchv = ph.sb("touchv", [P, 1])
        rz = ph.sb("rz", [P, GS])
        Vh = ph.sb("Vh", [P, QT_N, 32])
        Os = ph.sb("Os", [P, 2, GS * P])
        psS = ph.pb("psS", [P, N])
        psT = ph.pb("psT", [P, 2, N // 2])
        psO = ph.pb("psO", [P, 2, GS * P])
        psF = ph.pb("psF", [P, GS, P])
        (s_s, s_z, s_sub, s_t, s_exp, s_pv, s_vh, s_os, s_f, s_rz, s_div, s_clear) = (
            ph.sem(n) for n in "s z sub t exp pv vh os f rz div clear".split())
        if rel:
            EBT, scratch = rel
            rows = ph.sb("rows", [P, 4, BAND])
            psE = ph.pb("psE", [P, BAND])
            s_e, s_rows = ph.sem("e"), ph.sem("rows")
            s_wr = [ph.sem(f"wr{i}") for i in range(4)]
            s_bias = [ph.sem(f"bias{i}") for i in range(QT_N)]

        with nc.Block() as block:

            @block.tensor
            def _(pe):
                def scores(h, qt, u):
                    if not (type(u) is int and u == 0):
                        pe.wait_ge(s_z, u)
                    for var, k0, k1 in segments(qt):
                        kh = h if gkv == H else var * gkv + h // RPT
                        last = nc.tensor.matmul(psS[:, k0:k1], QT[0:KR, h, qt * P:(qt + 1) * P], KT[0:KR, kh, k0:k1],
                                                start=True, stop=True)
                    last.then_inc(s_s, 1)

                def relative(h, qt, v):
                    if not (type(v) is int and v == 0):
                        pe.wait_ge(s_rows, v)
                    nc.tensor.matmul(psE[:], QT[0:KR, h, qt * P:(qt + 1) * P], EBT[0:KR, :], start=True, stop=True).then_inc(s_e, 1)

                def values(h, qt, u, first):
                    g, t = qt // GS, qt % GS
                    if qt == 0:
                        pe.wait_ge(s_vh, h + 1)
                    if t == 0 and not first:
                        pe.wait_ge(s_os, h * 2 + (g - 1))
                    pe.wait_ge(s_exp, u * 2 + 2)
                    for kt in range(QT_N):
                        j = kt % 4
                        last = nc.tensor.matmul(psO[32 * j:32 * j + 32, g, t * P:(t + 1) * P], Vh[:, kt, :],
                                                Pt[:, qt % 2, kt * P:(kt + 1) * P], start=kt < 4, stop=kt >= 4)
                    last.then_inc(s_pv, 1)

                def to_rows(h, g, first=False):
                    pe.wait_ge(s_os, h * 2 + (g + 1))
                    if not first:
                        pe.wait_ge(s_div, h * 2 + g)
                    for t in range(GS):
                        last = nc.tensor.matmul(psF[:, t, 0:DH + 1], Os[:, g, t * P:(t + 1) * P], fold[:], start=True, stop=True)
                    last.then_inc(s_f, 1)

                def head(h, first=False, final=False):
                    for qt in range(QT_N):
                        u = h * QT_N + qt
                        pe.wait_ge(s_sub, u + 1)
                        for half in range(2):
                            if not (first and qt == 0):
                                pe.wait_ge(s_exp, u * 2 + (half - 1))
                            for k in range(4):
                                kt = half * 4 + k
                                last = nc.tensor.transpose(psT[:, half, k * P:(k + 1) * P], Z[:, qt % 2, kt * P:(kt + 1) * P], idf[:])
                            last.then_inc(s_t, 1)
                        if qt + 2 < QT_N:
                            scores(h, qt + 2, u + 2)
                        elif not final:
                            scores(h + 1, qt + 2 - QT_N, u + 2)
                        if rel and not final:
                            relative(h + 1, qt, u + QT_N)
                        if qt:
                            values(h, qt - 1, u - 1, first)
                        elif not first:
                            values(h - 1, QT_N - 1, u - 1, first)
                        if qt == 3 and not first:
                            to_rows(h - 1, 1)
                        if qt == 7:
                            to_rows(h, 0, first)

                if rel:
                    for qt in range(QT_N):
                        relative(0, qt, qt)
                scores(0, 0, 0)
                scores(0, 1, 1)
                head(0, first=True)
                with pe.Fori(1, H - 1) as h:
                    head(h)
                head(H - 1, final=True)
                values(H - 1, QT_N - 1, H * QT_N - 1, False)
                to_rows(H - 1, 1)

            @block.vector
            def _(dve):
                def copy_out(h, g):
                    dve.wait_ge(s_pv, h * QT_N + (g + 1) * GS)
                    nc.vector.tensor_copy(Os[:, g, :], psO[:, g, :]).then_inc(s_os, 1)

                def divide(h, g):
                    dve.wait_ge(s_f, h * 2 + (g + 1))
                    nc.vector.reciprocal(rz[:], psF[:, :, DH]).then_inc(s_rz, 1)
                    dve.wait_ge(s_rz, h * 2 + (g + 1))
                    nc.vector.tensor_tensor(attn[:, b * QT_N + g * GS:b * QT_N + (g + 1) * GS, bass.ts(h, DH)], psF[:, :, 0:DH],
                                            spread(rz[:].unsqueeze(2), [P, GS, DH]), ALU.mult).then_inc(s_div, 1)

                def head(h, first=False):
                    for qt in range(QT_N):
                        u = h * QT_N + qt
                        dve.wait_ge(s_s, u + 1)
                        nc.vector.memset(touch[:, 0, qt:qt + 1], 0.0)
                        if rel:
                            dve.wait_ge(s_bias[qt], h * 16 + 16)
                            nc.vector.memset(touch[:, 1, qt:qt + 1], 0.0)
                        nc.vector.tensor_tensor_reduce(out=Z[:, qt % 2, :], in0=psS[:], in1=A[:, qt, :], scale=1.0, scalar=3e38,
                                                       op0=ALU.add, op1=ALU.min, accum_out=m[:, qt % 2:qt % 2 + 1]).then_inc(s_z, 1)
                        if qt == 6:
                            copy_out(h, 0)
                        if not first:
                            if qt == 1:
                                divide(h - 1, 0)
                            if qt == 2:
                                copy_out(h - 1, 1)
                            if qt == 5:
                                divide(h - 1, 1)

                head(0, first=True)
                with dve.Fori(1, H) as h:
                    head(h)
                divide(H - 1, 0)
                copy_out(H - 1, 1)
                divide(H - 1, 1)

            @block.gpsimd
            def _(pool):
                nc.gpsimd.memset(Vh[:], 0.0).then_inc(s_clear, 1)
                pool.wait_ge(s_clear, 1)

                def head(h, first=False):
                    for qt in range(QT_N):
                        pool.wait_ge(s_z, h * QT_N + (qt + 1))
                        nc.gpsimd.tensor_tensor(touch[:, 2, qt:qt + 1], m[:, qt % 2:qt % 2 + 1], m[:, qt % 2:qt % 2 + 1], ALU.add)
                        nc.gpsimd.tensor_scalar(Z[:, qt % 2, :], Z[:, qt % 2, :], -1.0, m[:, qt % 2:qt % 2 + 1], ALU.mult, ALU.add).then_inc(s_sub, 1)
                        if qt == 1:
                            if not first:
                                pool.wait_ge(s_pv, h * QT_N)
                                nc.gpsimd.tensor_tensor(touchv[:], Vh[:, 0, 31:32], Vh[:, 0, 31:32], ALU.add)
                            nc.gpsimd.tensor_copy(Vh[:, :, 0:DH + 1], V[:, :, h if gkv == H else h // RPT, :]).then_inc(s_vh, 1)

                head(0, first=True)
                with pool.Fori(1, H) as h:
                    head(h)

            @block.scalar
            def _(act):
                def gather(v, slot, reuse):
                    if reuse is not None:
                        act.wait_ge(s_wr[slot], reuse)
                    act.wait_ge(s_e, v + 1)
                    nc.scalar.activation(rows[:, slot, :], psE[:], ACT.Copy).then_inc(s_rows, 1)

                def head(h, final=False):
                    for qt in range(QT_N):
                        u = h * QT_N + qt
                        for half in range(2):
                            act.wait_ge(s_t, u * 2 + (half + 1))
                            nc.scalar.activation(Pt[:, qt % 2, half * (N // 2):(half + 1) * (N // 2)], psT[:, half, :],
                                                 ACT.Exp).then_inc(s_exp, 1)
                        if rel and not final:
                            gather(u + QT_N, qt % 4, h * 32 + (32 if qt < 4 else 48))

                if rel:
                    for qt in range(QT_N):
                        gather(qt, qt % 4, 16 if qt >= 4 else None)
                with act.Fori(0, H - 1) as h:
                    head(h)
                head(H - 1, final=True)

            if rel:
                @block.sync
                def _(sp):
                    def store(h, qt):
                        sp.wait_ge(s_rows, h * QT_N + (qt + 1))
                        sp.dma_start(scratch[qt], rows[:, qt % 4, :]).then_inc(s_wr[qt % 4], 16)

                    def fetch(h, qt):
                        sp.wait_ge(s_wr[qt % 4], h * 32 + (16 if qt < 4 else 32))
                        lo, hi = max(qt - 1, 0), min(qt + 2, QT_N)
                        src = scratch[qt]
                        skew = bass.AP(src.tensor, src.offset + 255 - P * (qt - lo), [[BAND - 1, P], [1, (hi - lo) * P]])
                        sp.dma_start(A[:, qt, lo * P:hi * P], skew).then_inc(s_bias[qt], 16)

                    def head(h, first=False):
                        for qt in range(QT_N):
                            store(h, qt)
                            if qt >= 2:
                                fetch(h, qt - 2)
                            elif not first:
                                fetch(h - 1, qt - 2 + QT_N)

                    head(0, first=True)
                    with sp.Fori(1, H) as h:
                        head(h)
                    for qt in (QT_N - 2, QT_N - 1):
                        fetch(H - 1, qt)
                    for qt in range(QT_N):
                        sp.wait_ge(s_bias[qt], 16 * H)


def output_projection(nc, tag, attn, w, y, idf, residual=None, bias=None):
    with phase(nc, tag) as ph:
        aT = ph.sb("aT", [P, 2, CH])
        psT = ph.pb("psT", [P, 2, CH])
        psY = ph.pb("psY", [P, 2, TC, C])
        s_t, s_aT, s_y, s_out, s_own = (ph.sem(n) for n in "t aT y out own".split())
        with nc.Block() as block:

            @block.tensor
            def _(pe):
                for g in range(NCH + 1):
                    if g < NCH:
                        for t in range(TC):
                            last = nc.tensor.transpose(psT[:, g % 2, t * P:(t + 1) * P], attn[:, g * TC + t, :], idf[:])
                        last.then_inc(s_t, 1)
                    if g:
                        pe.wait_ge(s_aT, g)
                        if g >= 3:
                            pe.wait_ge(s_out, g - 2)
                        for t in range(TC):
                            last = nc.tensor.matmul(psY[:, (g - 1) % 2, t, :], aT[:, (g - 1) % 2, t * P:(t + 1) * P], w[:],
                                                    start=True, stop=True)
                        last.then_inc(s_y, 1)

            @block.scalar
            def _(act):
                for g in range(NCH):
                    act.wait_ge(s_t, g + 1)
                    if g >= 2:
                        act.wait_ge(s_y, g - 1)
                    nc.scalar.activation(aT[:, g % 2, :], psT[:, g % 2, :], ACT.Copy).then_inc(s_aT, 1)

            @block.vector
            def _(dve):
                own = Chain(dve, s_own)
                if bias is not None:
                    own(nc.vector.tensor_tensor(residual[:], residual[:], spread(bias[:].unsqueeze(1), [P, NT, C]), ALU.add))
                for g in range(NCH):
                    dve.wait_ge(s_y, g + 1)
                    out = y[:, g * TC:(g + 1) * TC, :]
                    if residual is None:
                        nc.vector.tensor_copy(out, psY[:, g % 2]).then_inc(s_out, 1)
                    else:
                        nc.vector.tensor_tensor(out, psY[:, g % 2], residual[:, g * TC:(g + 1) * TC, :], ALU.add).then_inc(s_out, 1)


def to_columns(nc, tag, xn, hT, idf, router=None, logits=None):
    with phase(nc, tag) as ph:
        psT = ph.pb("psT", [P, 2, CH])
        psL = ph.pb("psL", [P, NT, E])
        s_t, s_h, s_l, s_done = (ph.sem(n) for n in "t h l done".split())
        with nc.Block() as block:

            @block.tensor
            def _(pe):
                for g in range(NCH):
                    if g >= 2:
                        pe.wait_ge(s_h, g - 1)
                    for t in range(TC):
                        last = nc.tensor.transpose(psT[:, g % 2, t * P:(t + 1) * P], xn[:, g * TC + t, :], idf[:])
                    last.then_inc(s_t, 1)
                if router is not None:
                    pe.wait_ge(s_h, NCH)
                    for t in range(NT):
                        last = nc.tensor.matmul(psL[:, t, :], hT[:, t * P:(t + 1) * P], router[:], start=True, stop=True)
                    last.then_inc(s_l, 1)

            @block.scalar
            def _(act):
                for g in range(NCH):
                    act.wait_ge(s_t, g + 1)
                    nc.scalar.activation(hT[:, g * CH:(g + 1) * CH], psT[:, g % 2, :], ACT.Copy).then_inc(s_h, 1)

            if router is not None:
                @block.vector
                def _(dve):
                    dve.wait_ge(s_l, 1)
                    nc.vector.tensor_copy(logits[:], psL[:]).then_inc(s_done, 1)


def route(nc, tag, logits, kw, con):
    full = [P, NT, E]
    flat = "p t e -> p (t e)"
    with phase(nc, tag) as ph:
        p, pick, cand, w, sel, key = (ph.sb(n, full) for n in "p pick cand w sel key".split())
        r = ph.sb("r", [P, NT])
        r2 = ph.sb("r2", [P, NT])
        wide = ph.sb("wide", [P, NT, E, HI])
        col = ph.sb("col", [P, TOK])
        junk = ph.sb("junk", [P, TOK])
        ok, thr, cnt, hot, lo, unit, step, tmp = (ph.sb(n, [P, 1]) for n in "ok thr cnt hot lo unit step tmp".split())
        thrw = ph.sb("thrw", [P, P])
        thrt = ph.sb("thrt", [P, E])
        gt, eq = ph.sb("gt", full), ph.sb("eq", full)
        gtb, eqb = ph.sb("gtb", full, BF16), ph.sb("eqb", full, BF16)
        tot = ph.sb("tot", [P, 2, E, NT])
        acc = ph.sb("acc", [P, 2, E, NT])
        left = ph.sb("left", [P, E])
        rank = ph.sb("rank", full)
        psW = ph.pb("psW", [P, TOK])
        psN = ph.pb("psN", [P, 512])
        psR = ph.pb("psR", [P, 2, NT * E])
        psG = ph.pb("psG", [P, NT * E])
        s_own, s_exp, s_arg, s_wide, s_col, s_ok, s_n, s_thr, s_cmp, s_pre = (
            ph.sem(n) for n in "own exp arg wide col ok n thr cmp pre".split())
        rev, jfac, onehot0, blk, sub, ones, sel16 = (con[n] for n in "rev jfac j blk below ones sel16".split())
        STAGES = 8
        with nc.Block() as block:

            @block.vector
            def _(dve):
                v = nc.vector
                own = Chain(dve, s_own)
                ew = lambda a: spread(a[:].unsqueeze(2), full)
                own(v.reduce_max(r[:], logits[:], AX))
                v.tensor_tensor(p[:], logits[:], ew(r), ALU.subtract).then_inc(s_arg, 1)
                dve.wait_ge(s_exp, 1)
                own(v.reduce_sum(r[:], p[:], AX))
                own(v.reciprocal(r[:], r[:]))
                own(v.tensor_tensor(p[:], p[:], ew(r), ALU.mult))
                own(v.tensor_copy(cand[:], p[:]))
                for k in range(TOPK):
                    own(v.reduce_max(r[:], cand[:], AX))
                    own(v.tensor_tensor(pick[:], cand[:], ew(r), ALU.is_equal))
                    own(v.tensor_tensor(pick[:], pick[:], spread(rev[:].unsqueeze(1), full), ALU.mult))
                    own(v.reduce_max(r[:], pick[:], AX))
                    own(v.tensor_tensor(pick[:], pick[:], ew(r), ALU.is_equal))
                    if k == 0:
                        own(v.tensor_copy(sel[:], pick[:]))
                    else:
                        own(v.tensor_tensor(sel[:], sel[:], pick[:], ALU.add))
                    own(v.scalar_tensor_tensor(out=cand[:], in0=pick[:], scalar=-4.0, in1=cand[:], op0=ALU.mult, op1=ALU.add))
                own(v.tensor_tensor(w[:], p[:], sel[:], ALU.mult))
                own(v.reduce_sum(r[:], w[:], AX))
                own(v.tensor_scalar(r[:], r[:], EPS_MOE, None, ALU.max))
                own(v.reciprocal(r[:], r[:]))
                own(v.tensor_tensor(w[:], w[:], ew(r), ALU.mult))
                own(v.tensor_scalar(cand[:], sel[:], -1.0, None, ALU.add))
                own(v.tensor_tensor(key[:], w[:], cand[:], ALU.add))
                v.tensor_copy(wide[:], spread(key[:].unsqueeze(3), [P, NT, E, HI])).then_inc(s_wide, 1)
                dve.wait_ge(s_col, 1)
                own(v.tensor_copy(col[:], psW[:]))
                for st in range(STAGES):
                    if st == 0:
                        own(v.tensor_copy(thr[:], jfac[:, 0:1]))
                    elif st == 1:
                        own(v.tensor_tensor(thr[:], lo[:], jfac[:, 1:2], ALU.mult))
                    else:
                        shift = 2.0 ** -4 if st < STAGES - 1 else 2.0 ** -3
                        if st == 2:
                            own(v.tensor_scalar(step[:], lo[:], shift, None, ALU.mult))
                        else:
                            own(v.tensor_scalar(step[:], step[:], shift, None, ALU.mult))
                        own(v.scalar_tensor_tensor(out=thr[:], in0=step[:], scalar=onehot0[:, 0:1], in1=lo[:], op0=ALU.mult, op1=ALU.add))
                    own(v.tensor_scalar(junk[:], col[:], thr[:, 0:1], None, ALU.is_ge, ALU.add, accum_out=cnt[:, 0:1]))
                    v.tensor_scalar(ok[:], cnt[:], float(CAP), None, ALU.is_ge).then_inc(s_ok, 1)
                    dve.wait_ge(s_n, 2 * st + 1 if st < 2 else st + 3)
                    if st < 2:
                        own(v.tensor_scalar(hot[:], psN[:, 0:1], onehot0[:, 0:1], -1.0, ALU.subtract, ALU.add))
                        own(v.tensor_scalar(hot[:], hot[:], 0.0, None, ALU.is_equal))
                        v.tensor_tensor(hot[:], hot[:], thr[:], ALU.mult).then_inc(s_ok, 1)
                        dve.wait_ge(s_n, 2 * st + 2)
                        own(v.tensor_copy(lo[:], psN[:, 0:1]))
                    else:
                        own(v.tensor_scalar(tmp[:], psN[:, 0:1], -1.0, None, ALU.add))
                        own(v.scalar_tensor_tensor(out=lo[:], in0=tmp[:], scalar=step[:, 0:1], in1=lo[:], op0=ALU.mult, op1=ALU.add))
                v.tensor_copy(thrw[:], spread(lo[:], [P, P])).then_inc(s_thr, 1)
                dve.wait_ge(s_n, STAGES + 3)
                own(v.tensor_copy(thrt[:], psN[:, 0:E]))
                te = spread(thrt[:].unsqueeze(1), full)
                own(v.tensor_tensor(gt[:], key[:], te, ALU.is_gt))
                own(v.tensor_tensor(eq[:], key[:], te, ALU.is_equal))
                own(v.tensor_copy(gtb[:], gt[:]))
                v.tensor_copy(eqb[:], eq[:]).then_inc(s_cmp, 1)
                dve.wait_ge(s_pre, 1)
                own(v.tensor_copy(tot[:, 0], psG[:].rearrange("p (t e) -> p e t", e=E)))
                own(v.reduce_sum(left[:], tot[:, 0], AX))
                own(v.tensor_scalar(left[:], left[:], -1.0, float(CAP), ALU.mult, ALU.add))
                own(v.tensor_copy(acc[:, 0], psR[:, 1, :].rearrange("p (t e) -> p e t", e=E)))
                own(v.tensor_copy(tot[:, 1], acc[:, 0]))
                a, k = 0, 1
                while k < NT:
                    own(v.tensor_copy(acc[:, 1 - a, :, 0:k], acc[:, a, :, 0:k]))
                    own(v.tensor_tensor(acc[:, 1 - a, :, k:NT], acc[:, a, :, k:NT], acc[:, a, :, 0:NT - k], ALU.add))
                    a, k = 1 - a, 2 * k
                own(v.tensor_tensor(acc[:, a], acc[:, a], tot[:, 1], ALU.subtract))
                own(v.tensor_tensor(rank[:], psR[:, 0, :].rearrange("p (t e) -> p t e", e=E), acc[:, a].rearrange("p e t -> p t e"), ALU.add))
                own(v.tensor_tensor(rank[:], rank[:], spread(left[:].unsqueeze(1), full), ALU.is_lt))
                own(v.tensor_tensor(eq[:], eq[:], rank[:], ALU.mult))
                own(v.tensor_tensor(gt[:], gt[:], eq[:], ALU.add))
                own(v.tensor_tensor(w[:], w[:], gt[:], ALU.mult))
                own(v.tensor_tensor(w[:], w[:], sel[:], ALU.mult))
                own(v.reduce_sum(r2[:], w[:], AX))
                own(v.tensor_scalar(r2[:], r2[:], EPS_MOE, None, ALU.max))
                own(v.reciprocal(r2[:], r2[:]))
                own(v.tensor_tensor(kw[:], w[:], ew(r2), ALU.mult))

            @block.scalar
            def _(act):
                act.wait_ge(s_arg, 1)
                nc.scalar.activation(p[:], p[:], ACT.Exp).then_inc(s_exp, 1)

            @block.tensor
            def _(pe):
                pe.wait_ge(s_wide, 1)
                for t in range(NT):
                    last = nc.tensor.transpose(psW[:, t * P:(t + 1) * P], wide[:, t].rearrange("p e j -> p (e j)"), con["idf"][:])
                last.then_inc(s_col, 1)
                n = 0
                for st in range(STAGES):
                    n += 1
                    pe.wait_ge(s_ok, n)
                    nc.tensor.matmul(psN[:, 0:1], blk[:], ok[:], start=True, stop=True).then_inc(s_n, 1)
                    if st < 2:
                        n += 1
                        pe.wait_ge(s_ok, n)
                        nc.tensor.matmul(psN[:, 0:1], blk[:], hot[:], start=True, stop=True).then_inc(s_n, 1)
                pe.wait_ge(s_thr, 1)
                nc.tensor.matmul(psN[:, 0:E], thrw[:], sel16[:], start=True, stop=True).then_inc(s_n, 1)
                pe.wait_ge(s_cmp, 1)
                nc.tensor.matmul(psG[:], ones[:], gtb[:].rearrange(flat), start=True, stop=True)
                nc.tensor.matmul(psR[:, 0, :], sub[:], eqb[:].rearrange(flat), start=True, stop=True)
                nc.tensor.matmul(psR[:, 1, :], ones[:], eqb[:].rearrange(flat), start=True, stop=True).then_inc(s_pre, 1)


def experts(nc, tag, hT, kw, acc, wp, wg, wo):
    with phase(nc, tag) as ph:
        WP, WG = ph.sb("WP", [P, 2, DFF]), ph.sb("WG", [P, 2, DFF])
        WO = ph.sb("WO", [P, 2, FT, C])
        sg = ph.sb("sg", [P, 2, CH])
        y = ph.sb("y", [P, 2, FT, CH])
        psP, psG = ph.pb("psP", [P, 2, CH]), ph.pb("psG", [P, 2, CH])
        psO = ph.pb("psO", [P, 2, TC, C])
        s_w = [ph.sem("w0"), ph.sem("w1")]
        s_pg, s_sg, s_y, s_o, s_acc, s_used, s_zero = (ph.sem(n) for n in "pg sg y o acc used zero".split())
        with nc.Block() as block:

            @block.sync
            def _(sp):
                def load(e, s):
                    sp.dma_start(WP[:, s, :], wp[e]).then_inc(s_w[s], 16)
                    sp.dma_start(WG[:, s, :], wg[e]).then_inc(s_w[s], 16)
                    sp.dma_start(WO[:, s], wo[e].rearrange("(f p) h -> p f h", p=P)).then_inc(s_w[s], 16)

                load(0, 0)
                load(1, 1)
                with sp.Fori(1, E // 2) as i:
                    for s in range(2):
                        sp.wait_ge(s_used, i * 2 + (s - 1))
                        load(i * 2 + s, s)

            @block.tensor
            def _(pe):
                def hidden(i, s, c, f):
                    k = i * 32 + (s * 16 + c * 4 + f)
                    if not (type(i) is int and k < 2):
                        pe.wait_ge(s_y, k - 1)
                    cols = hT[:, c * CH:(c + 1) * CH]
                    nc.tensor.matmul(psP[:, f % 2, :], WP[:, s, f * P:(f + 1) * P], cols, start=True, stop=True)
                    nc.tensor.matmul(psG[:, f % 2, :], WG[:, s, f * P:(f + 1) * P], cols, start=True, stop=True).then_inc(s_pg, 1)

                def back(i, s, c):
                    q = i * 8 + (s * 4 + c)
                    pe.wait_ge(s_y, q * 4 + 4)
                    if not (type(i) is int and q < 2):
                        pe.wait_ge(s_acc, q * 4 - 4)
                    for t in range(TC):
                        for f in range(FT):
                            last = nc.tensor.matmul(psO[:, c % 2, t, :], y[:, c % 2, f, t * P:(t + 1) * P], WO[:, s, f, :],
                                                    start=f == 0, stop=f == FT - 1)
                    last.then_inc(s_o, 1)
                    if c == NCH - 1:
                        pe.sem_inc(s_used, 0) if False else None

                def pair(i, first=False):
                    for s in range(2):
                        pe.wait_ge(s_w[s], i * 48 + 48)
                        for c in range(NCH):
                            for f in range(FT):
                                hidden(i, s, c, f)
                                if f == 1:
                                    if c:
                                        back(i, s, c - 1)
                                    elif s:
                                        back(i, 0, NCH - 1)
                                    elif not first:
                                        back(i - 1, 1, NCH - 1)

                pair(0, first=True)
                with pe.Fori(1, E // 2) as i:
                    pair(i)
                back(E // 2 - 1, 1, NCH - 1)

            @block.scalar
            def _(act):
                with act.Fori(0, E // 2) as i:
                    for k in range(32):
                        act.wait_ge(s_pg, i * 32 + (k + 1))
                        nc.scalar.activation(sg[:, k % 2, :], psG[:, k % 2, :], ACT.Silu).then_inc(s_sg, 1)

            @block.vector
            def _(dve):
                nc.vector.memset(acc[:], 0.0).then_inc(s_zero, 1)
                dve.wait_ge(s_zero, 1)

                def add(i, s, c):
                    q = i * 8 + (s * 4 + c)
                    dve.wait_ge(s_o, q + 1)
                    for t in range(TC):
                        n = c * TC + t
                        nc.vector.scalar_tensor_tensor(
                            out=acc[:, n, :], in0=psO[:, c % 2, t, :], scalar=kw[:, n, bass.ds(i * 2 + s, 1)],
                            in1=acc[:, n, :], op0=ALU.mult, op1=ALU.add).then_inc(s_acc, 1)
                    if c == NCH - 1:
                        nc.vector.engine_nop().then_inc(s_used, 1)

                def pair(i, first=False):
                    for s in range(2):
                        for c in range(NCH):
                            for f in range(FT):
                                k = i * 32 + (s * 16 + c * 4 + f)
                                dve.wait_ge(s_sg, k + 1)
                                nc.vector.tensor_tensor(y[:, c % 2, f, :], psP[:, f % 2, :], sg[:, f % 2, :], ALU.mult).then_inc(s_y, 1)
                                if f == 3:
                                    if c:
                                        add(i, s, c - 1)
                                    elif s:
                                        add(i, 0, NCH - 1)
                                    elif not first:
                                        add(i - 1, 1, NCH - 1)

                pair(0, first=True)
                with dve.Fori(1, E // 2) as i:
                    pair(i)
                add(E // 2 - 1, 1, NCH - 1)


def compose(nc, tag, W1, W2, primitives, logit_rows, logit_all):
    with phase(nc, tag) as ph:
        (A1, s_a1), (B1, s_b1), (A2, s_a2), (B2, s_b2) = primitives
        lr, la = ph.sb("lr", [P, 2, KT_C]), ph.sb("la", [P, 2, 32])
        mx, sm = ph.sb("mx", [P, 2]), ph.sb("sm", [P, 2])
        ps1, ps2 = ph.pb("ps1", [P, DFF]), ph.pb("ps2", [P, FT, 512])
        s_l, s_own, s_arg, s_exp, s_sc, s_mm, s_done = (ph.sem(n) for n in "l own arg exp sc mm done".split())
        with nc.Block() as block:

            @block.sync
            def _(sp):
                sp.dma_start(lr[:], logit_rows).then_inc(s_l, 16)
                sp.dma_start(la[:], logit_all).then_inc(s_l, 16)

            @block.vector
            def _(dve):
                v = nc.vector
                own = Chain(dve, s_own)
                dve.wait_ge(s_l, 32)
                own(v.reduce_max(mx[:], la[:], AX))
                own(v.tensor_tensor(la[:], la[:], spread(mx[:].unsqueeze(2), [P, 2, 32]), ALU.subtract))
                v.tensor_tensor(lr[:], lr[:], spread(mx[:].unsqueeze(2), [P, 2, KT_C]), ALU.subtract).then_inc(s_arg, 1)
                dve.wait_ge(s_exp, 2)
                own(v.reduce_sum(sm[:], la[:], AX))
                own(v.reciprocal(sm[:], sm[:]))
                own(v.tensor_tensor(lr[:], lr[:], spread(sm[:].unsqueeze(2), [P, 2, KT_C]), ALU.mult))
                dve.wait_ge(s_a1, 16)
                v.tensor_tensor(A1[:], A1[:], spread(lr[:, 0].unsqueeze(2), [P, KT_C, C]), ALU.mult).then_inc(s_sc, 1)
                dve.wait_ge(s_b2, 16)
                v.tensor_tensor(B2[:], B2[:], spread(lr[:, 1].unsqueeze(2), [P, KT_C, C]), ALU.mult).then_inc(s_sc, 1)
                dve.wait_ge(s_mm, 1)
                v.tensor_copy(W1[:], ps1[:]).then_inc(s_done, 1)
                dve.wait_ge(s_mm, 2)
                v.tensor_copy(W2[:], ps2[:, :, 0:C]).then_inc(s_done, 1)

            @block.scalar
            def _(act):
                act.wait_ge(s_arg, 1)
                nc.scalar.activation(la[:], la[:], ACT.Exp).then_inc(s_exp, 1)
                nc.scalar.activation(lr[:], lr[:], ACT.Exp).then_inc(s_exp, 1)

            @block.tensor
            def _(pe):
                pe.wait_ge(s_sc, 1)
                pe.wait_ge(s_b1, 16)
                for k in range(KT_C):
                    last = nc.tensor.matmul(ps1[:], A1[:, k, :], B1[:, k, :], start=k == 0, stop=k == KT_C - 1)
                last.then_inc(s_mm, 1)
                pe.wait_ge(s_sc, 2)
                pe.wait_ge(s_a2, 16)
                for f in range(FT):
                    for k in range(KT_C):
                        last = nc.tensor.matmul(ps2[:, f, 0:C], A2[:, k, f * P:(f + 1) * P], B2[:, k, :],
                                                start=k == 0, stop=k == KT_C - 1)
                last.then_inc(s_mm, 1)


def feed_forward(nc, tag, hT, W1, W2, y):
    with phase(nc, tag) as ph:
        g = ph.sb("g", [P, 2, FT, CH])
        psH = ph.pb("psH", [P, 2, CH])
        psY = ph.pb("psY", [P, 2, TC, C])
        s_h, s_g, s_y, s_out = (ph.sem(n) for n in "h g y out".split())
        with nc.Block() as block:

            @block.tensor
            def _(pe):
                for c in range(NCH + 1):
                    if c < NCH:
                        for f in range(FT):
                            k = c * FT + f
                            if k >= 2:
                                pe.wait_ge(s_g, k - 1)
                            nc.tensor.matmul(psH[:, f % 2, :], W1[:, f * P:(f + 1) * P], hT[:, c * CH:(c + 1) * CH],
                                             start=True, stop=True).then_inc(s_h, 1)
                    if c:
                        pe.wait_ge(s_g, c * FT)
                        if c >= 3:
                            pe.wait_ge(s_out, c - 2)
                        for t in range(TC):
                            for f in range(FT):
                                last = nc.tensor.matmul(psY[:, (c - 1) % 2, t, :], g[:, (c - 1) % 2, f, t * P:(t + 1) * P], W2[:, f, :],
                                                        start=f == 0, stop=f == FT - 1)
                        last.then_inc(s_y, 1)

            @block.scalar
            def _(act):
                for c in range(NCH):
                    if c >= 2:
                        act.wait_ge(s_y, c - 1)
                    for f in range(FT):
                        act.wait_ge(s_h, c * FT + f + 1)
                        nc.scalar.activation(g[:, c % 2, f, :], psH[:, f % 2, :], ACT.Gelu_apprx_tanh).then_inc(s_g, 1)

            @block.vector
            def _(dve):
                for c in range(NCH):
                    dve.wait_ge(s_y, c + 1)
                    nc.vector.tensor_copy(y[:, c * TC:(c + 1) * TC, :], psY[:, c % 2]).then_inc(s_out, 1)


def sandwich(nc: bass.Bass, x, wqkv0, wpre, bpre, wproj, bproj, pi, router, moe_pre, moe_gate, moe_post,
             wqkv1, wo1, far, band, a1, b1, a2, b2, logit_rows, logit_all, con_f, out):
    keep = ExitStack()
    sb = lambda name, shape, dt=F32: keep.enter_context(nc.sbuf_tensor(name, shape, dt))
    scratch = nc.dram_tensor("relative_rows", (QT_N, P, BAND), F32, kind="Internal").ap()
    x_rows = x.rearrange("(t p) c -> p t c", p=P)
    out_rows = out.rearrange("(t p) c -> p t c", p=P)
    X, y, hT = sb("X", [P, NT, C]), sb("y", [P, NT, C]), sb("hT", [P, TOK])
    W1, W2 = sb("W1", [P, DFF]), sb("W2", [P, FT, C])
    idf, idb = sb("idf", [P, P]), sb("idb", [P, P], BF16)
    blk, below, ones = sb("blk", [P, P]), sb("below", [P, P], BF16), sb("ones", [P, P], BF16)
    cf = sb("cf", [P, 3 + E + E + DH + 1])
    con = {"idf": idf, "blk": blk, "below": below, "ones": ones, "j": cf[:, 0:1], "jfac": cf[:, 1:3],
           "rev": cf[:, 3:3 + E], "sel16": cf[:, 3 + E:3 + 2 * E],
           "fold": cf[:, 3 + 2 * E:3 + 2 * E + DH + 1]}

    with phase(nc, "load") as ph:
        s_x, s_c, s_id = ph.sem("x"), ph.sem("c"), ph.sem("id")
        with nc.Block() as block:

            @block.sync
            def _(sp):
                sp.dma_start(X[:], x_rows).then_inc(s_x, 16)
                sp.dma_start(cf[:], con_f).then_inc(s_x, 16)
                sp.wait_ge(s_x, 32)

            @block.gpsimd
            def _(pool):
                g = nc.gpsimd
                n = 0
                for t, val in ((idf, 0.0), (idb, 0.0), (blk, 1.0), (below, 1.0), (ones, 1.0)):
                    g.memset(t[:], val).then_inc(s_id, 1)
                    n += 1
                pool.wait_ge(s_id, n)
                for t in (idf, idb):
                    g.affine_select(out=t[:], in_=t[:], compare_op=ALU.not_equal, fill=1.0, base=0,
                                    pattern=[[-1, P]], channel_multiplier=1).then_inc(s_id, 1)
                    n += 1
                g.affine_select(out=below[:], in_=below[:], compare_op=ALU.is_gt, fill=0.0, base=0,
                                pattern=[[1, P]], channel_multiplier=-1).then_inc(s_id, 1)
                n += 1
                view = blk[:].rearrange("p (a r) -> p a r", r=HI)
                g.affine_select(out=view, in_=view, compare_op=ALU.is_ge, fill=0.0, base=0,
                                pattern=[[-HI, P // HI], [0, HI]], channel_multiplier=1).then_inc(s_id, 1)
                n += 1
                pool.wait_ge(s_id, n)
                g.affine_select(out=view, in_=view, compare_op=ALU.is_gt, fill=0.0, base=HI,
                                pattern=[[HI, P // HI], [0, HI]], channel_multiplier=-1).then_inc(s_id, 1)
                pool.wait_ge(s_id, n + 1)

    with phase(nc, "a0") as ph:
        xn = ph.sb("xn", [P, NT, C])
        w, wp, wo = ph.sb("w", [P, 3 * C]), ph.sb("wp", [P, C]), ph.sb("wo", [P, C])
        bp, bo, npi = ph.sb("bp", [P, 1]), ph.sb("bo", [P, C]), ph.sb("npi", [P, 1])
        s_in, s_pi = ph.sem("in"), ph.sem("pi")
        with nc.Block() as block:

            @block.sync
            def _(sp):
                for dst, src in ((w, wqkv0), (wp, wpre), (wo, wproj), (bp, bpre), (bo, bproj), (npi, pi)):
                    sp.dma_start(dst[:], src).then_inc(s_in, 16)
                sp.wait_ge(s_in, 96)

            @block.vector
            def _(dve):
                dve.wait_ge(s_in, 96)
                nc.vector.tensor_scalar(npi[:], npi[:], -(C ** -0.5), None, ALU.mult).then_inc(s_pi, 1)
                dve.wait_ge(s_pi, 1)

        layer_norm(nc, "n0", X, dst=xn)
        for b in range(B):
            with phase(nc, f"a0b{b}") as pb_:
                QT, KT = pb_.sb("QT", [P, H, N], BF16), pb_.sb("KT", [P, H, N], BF16)
                V = pb_.sb("V", [P, QT_N, H, DH + 1])
                L = pb_.sb("L", [P, QT_N, N])
                preT = pb_.sb("preT", [P, N])
                s_one = pb_.sem("one")
                with nc.Block() as block:

                    @block.gpsimd
                    def _(pool):
                        nc.gpsimd.memset(V[:, :, :, DH:DH + 1], 1.0).then_inc(s_one, 1)
                        pool.wait_ge(s_one, 1)

                project(nc, f"p0{b}", b, xn, w, H, QT, KT, V, idf, idb, pre=(wp, bp, preT))
                shared_logits(nc, f"l0{b}", preT, npi, L)
                attend(nc, f"t0{b}", b, QT, KT, H, V, L, y, con, lambda qt: [(0, 0, 512), (0, 512, 1024)])
        output_projection(nc, "o0", y, wo, y, idf, residual=xn, bias=bo)
        layer_norm(nc, "m0", y, add_to=X)

    with phase(nc, "e") as ph:
        xn = ph.sb("xn", [P, NT, C])
        logits, kw = ph.sb("logits", [P, NT, E]), ph.sb("kw", [P, NT, E])
        rt = ph.sb("rt", [P, E])
        s_in = ph.sem("in")
        primitives = [(ph.sb(n, [P, KT_C, cols]), ph.sem(n)) for n, cols in (("A1", C), ("B1", DFF), ("A2", DFF), ("B2", C))]
        with nc.Block() as block:

            @block.sync
            def _(sp):
                sp.dma_start(rt[:], router).then_inc(s_in, 16)
                for (dst, sem), src in zip(primitives, (a1, b1, a2, b2)):
                    sp.dma_start(dst[:], src.rearrange("(k p) n -> p k n", p=P)).then_inc(sem, 16)
                sp.wait_ge(s_in, 16)

        layer_norm(nc, "n1", X, dst=xn)
        to_columns(nc, "c1", xn, hT, idf, router=rt, logits=logits)
        route(nc, "r1", logits, kw, con)
        experts(nc, "x1", hT, kw, y, moe_pre, moe_gate, moe_post)
        compose(nc, "w", W1, W2, primitives, logit_rows, logit_all)
        layer_norm(nc, "m1", y, add_to=X)

    GKV = far.shape[1] // (2 * DH)
    with phase(nc, "a1") as ph:
        xn = hT[:].rearrange("p (t c) -> p t c", c=C)
        w, wo = ph.sb("w", [P, wqkv1.shape[1]]), ph.sb("wo", [P, C])
        ef = ph.sb("ef", [P, 2, GKV * DH])
        eb = ph.sb("eb", [P, BAND // P, DH])
        ebp = ph.sb("ebp", [P, SPLIT, BAND // P, DH], BF16)
        ebx = ph.sb("ebx", [P, BAND // P, SPLIT, SPLIT, DH], BF16)
        EBT = ph.sb("EBT", [P, BAND], BF16)
        with phase(nc, "band") as pw:
            psB = pw.pb("psB", [P, BAND // P, P], BF16)
            s_in, s_own, s_x, s_t = (pw.sem(n) for n in "in own x t".split())
            with nc.Block() as block:

                @block.sync
                def _(sp):
                    for dst, src in ((eb[:], band.rearrange("(t p) d -> p t d", p=P)), (w[:], wqkv1), (wo[:], wo1),
                                     (ef[:], far.rearrange("p (a k) -> p a k", a=2))):
                        sp.dma_start(dst, src).then_inc(s_in, 16)
                    sp.wait_ge(s_in, 64)

                @block.vector
                def _(dve):
                    own = Chain(dve, s_own)
                    dve.wait_ge(s_in, 64)
                    split(nc, own, eb[:], ebp)
                    for j in range(SPLIT):
                        last = nc.vector.tensor_copy(ebx[:, :, :, j], spread(ebp[:, j].unsqueeze(2), [P, BAND // P, SPLIT, DH]))
                    last.then_inc(s_x, 1)
                    dve.wait_ge(s_t, 1)
                    own(nc.vector.tensor_copy(EBT[0:KR, :], psB[0:KR].rearrange("p t k -> p (t k)")))

                @block.tensor
                def _(pe):
                    pe.wait_ge(s_x, 1)
                    for t in range(BAND // P):
                        last = nc.tensor.transpose(psB[0:KR, t, :], ebx[:, t].rearrange("p i j d -> p (i j d)"), idb[:])
                    last.then_inc(s_t, 1)

        layer_norm(nc, "n2", X, dst=xn)

        def segments(qt):
            cuts = [0, max(qt - 1, 0) * P, min(qt + 2, QT_N) * P, N]
            found = []
            for var, k0, k1 in ((1, cuts[0], cuts[1]), (0, cuts[1], cuts[2]), (2, cuts[2], cuts[3])):
                for a, z in ((k0, min(k1, 512)), (max(k0, 512), k1)):
                    if a < z:
                        found.append((var, a, z))
            return found

        for b in range(B):
            with phase(nc, f"a1b{b}") as pb_:
                QT, KT = pb_.sb("QT", [P, H, N], BF16), pb_.sb("KT", [P, 3 * GKV, N], BF16)
                V = pb_.sb("V", [P, QT_N, GKV, DH + 1])
                A = pb_.sb("A", [P, QT_N, N])
                s_one, s_zero = pb_.sem("one"), pb_.sem("zero")
                with nc.Block() as block:

                    @block.gpsimd
                    def _(pool):
                        nc.gpsimd.memset(V[:, :, :, DH:DH + 1], 1.0).then_inc(s_one, 1)
                        pool.wait_ge(s_one, 1)

                    @block.vector
                    def _(dve):
                        nc.vector.memset(A[:], 0.0).then_inc(s_zero, 1)
                        dve.wait_ge(s_zero, 1)

                project(nc, f"p1{b}", b, xn, w, GKV, QT, KT, V, idf, idb, efar=ef)
                attend(nc, f"t1{b}", b, QT, KT, GKV, V, A, y, con, segments, rel=(EBT, scratch))
        output_projection(nc, "o1", y, wo, y, idf)
        layer_norm(nc, "m2", y, add_to=X)

    with phase(nc, "f") as ph:
        xn = ph.sb("xn", [P, NT, C])
        layer_norm(nc, "n3", X, dst=xn)
        to_columns(nc, "c3", xn, hT, idf)
        feed_forward(nc, "g3", hT, W1, W2, y)
        layer_norm(nc, "m3", y, add_to=X)

    with phase(nc, "store") as ph:
        s_out = ph.sem("out")
        with nc.Block() as block:

            @block.sync
            def _(sp):
                sp.dma_start(out_rows, X[:]).then_inc(s_out, 16)
                sp.wait_ge(s_out, 16)
    keep.close()


def kernel(**inputs):
    import numpy as np
    import concourse.bacc as bacc
    from concourse.bass_utils import run_bass_kernel_spmd as run

    a = {k: np.asarray(v) for k, v in inputs.items()}
    heads = a["L1_attn_E"].shape[1]
    rel = a["L1_attn_E"]
    last = rel.shape[0] - 1
    band = rel[np.clip(255 - np.arange(BAND), -(last // 2), last // 2) + last // 2]
    groups = a["L1_attn_Wk"].shape[0] // heads
    far = np.concatenate([np.tile(rel[last], groups), np.tile(rel[0], groups)])
    row = lambda v: np.broadcast_to(v, (P, v.size))
    j = np.tile(np.arange(HI, dtype=np.float32), P // HI)
    consts = np.zeros((P, 3 + 2 * E + heads + 1), np.float32)
    consts[:, 0] = j
    consts[:, 1] = 2.0 ** (8 * j - 126)
    consts[:, 2] = 2.0 ** np.minimum(j, 8)
    consts[:, 3:3 + E] = E - np.arange(E)
    consts[np.arange(E) * HI, 3 + E + np.arange(E)] = 1.0
    for q in range(4):
        consts[32 * q + np.arange(heads + 1), 3 + 2 * E + np.arange(heads + 1)] = 1.0
    rank = lambda v: v.transpose(0, 2, 1).reshape(RANK_ROWS, -1)
    lg = [a["L1_ffn_fc1_logits"], a["L1_ffn_fc2_logits"]]
    per = RANK_ROWS // lg[0].size
    ins = {
        "x": a["L0_attn_x"].reshape(TOK, C),
        "wqkv0": np.concatenate([a["L0_attn_Wq"], a["L0_attn_Wk"], a["L0_attn_Wv"]], 1),
        "wpre": a["L0_attn_Wpre"], "bpre": a["L0_attn_bpre"].reshape(C, 1),
        "wproj": a["L0_attn_Wproj"], "bproj": row(a["L0_attn_bproj"]), "pi": row(a["L0_attn_pi"]),
        "router": a["L0_ffn_router_weight"].T,
        "moe_pre": a["L0_ffn_ff_pre_act_weight"].transpose(0, 2, 1),
        "moe_gate": a["L0_ffn_gate_weight"].transpose(0, 2, 1),
        "moe_post": a["L0_ffn_ff_post_act_weight"].transpose(0, 2, 1),
        "wqkv1": np.concatenate([a["L1_attn_Wq"], a["L1_attn_Wk"], a["L1_attn_Wv"]], 0).T,
        "wo1": a["L1_attn_Wo"].T, "far": row(far), "band": band,
        "a1": rank(a["L1_ffn_fc1_A"]), "b1": a["L1_ffn_fc1_B"].reshape(RANK_ROWS, -1),
        "a2": rank(a["L1_ffn_fc2_A"]), "b2": a["L1_ffn_fc2_B"].reshape(RANK_ROWS, -1),
        "logit_rows": np.stack([np.repeat(v, per).reshape(KT_C, P).T for v in lg], 1),
        "logit_all": np.stack([row(v) for v in lg], 1),
        "con_f": consts,
    }
    nc = bacc.Bacc("TRN2", target_bir_lowering=False, num_devices=1)
    arrays, args = {}, []
    for name, v in ins.items():
        v = np.ascontiguousarray(v)
        arrays[f"in_{name}"] = v
        args.append(nc.dram_tensor(f"in_{name}", v.shape, mybir.dt.from_np(v.dtype), kind="ExternalInput").ap())
    args.append(nc.dram_tensor("out_x", (TOK, C), F32, kind="ExternalOutput").ap())
    sandwich(nc, *args)
    r = run(nc, [arrays], core_ids=[0])
    return r.results[0]["out_x"].reshape(B, N, C)
```
